# Optimizing a Trainium2 kernel written in Bass

```python
import numpy as np
import jax
import jax.numpy as jnp

def _softmax(x, axis=-1):
    return jax.nn.softmax(x, axis=axis)

def _gelu(x):
    return jax.nn.gelu(x, approximate=True)

def _silu(x):
    return jax.nn.silu(x)

def _sigmoid(x):
    return jax.nn.sigmoid(x)

def _layernorm(x, axis=-1, eps=1e-05):
    m = jnp.mean(x, axis=axis, keepdims=True)
    v = jnp.var(x, axis=axis, keepdims=True)
    return (x - m) / jnp.sqrt(v + eps)

def _scatter_add(tgt, idx, src, axis=0):
    return tgt.at[idx].add(src)

def _segment_sum(src, seg, n):
    return jax.ops.segment_sum(src, seg, n)
kernel_name = 'mk_cond_resid_d2_seqx_r2_fda650'

def setup_inputs(seed: int=0):
    np.random.seed(seed)
    _w = jnp.asarray

    def _rec_inputs():
        import jax
        import jax.numpy as jnp
        _rk = jax.random.key(seed)
        x = -0.000125 + 0.9999 * jax.random.normal(jax.random.fold_in(_rk, 1), (32, 512, 512), jnp.float32)
        _lenS = 512 - jax.random.randint(jax.random.fold_in(_rk, 7), (32,), 0, max(1, 512 // 4) + 1, jnp.int32)
        _lenS2 = 512 - jax.random.randint(jax.random.fold_in(_rk, 8), (32,), 0, max(1, 512 // 4) + 1, jnp.int32)
        cond_1024 = 0.00513981 + 1.0024 * jax.random.normal(jax.random.fold_in(_rk, 11), (32, 512), jnp.float32)
        return (x, cond_1024)
    x, cond_1024 = _rec_inputs()

    def _L0_cond_setup():
        import jax, jax.numpy as jnp
        import numpy as np
        IN_FEATURES = 512
        OUT_FEATURES = 512
        BATCH = 32
        SEQ = 512
        EPS = 1e-08
        key = jax.random.key(seed)
        k1, k2, k3 = jax.random.split(key, 3)
        Efou = jax.random.normal(k1, (BATCH, SEQ, IN_FEATURES), dtype=jnp.float32)
        y = jax.random.normal(k2, (BATCH, IN_FEATURES), dtype=jnp.float32)
        weight = jax.random.normal(k3, (IN_FEATURES, OUT_FEATURES), dtype=jnp.float32)
        return {'Efou': Efou, 'y': y, 'weight': weight}
    _L0_cond_all = _L0_cond_setup()
    _L0_cond_in = {k: v for k, v in _L0_cond_all.items() if k in ('weight',)}
    del _L0_cond_all

    def _L1_cond_setup():
        import jax, jax.numpy as jnp
        import numpy as np
        N, T, D, H = (64, 256, 512, 512)
        key = jax.random.key(seed)
        k1, k2, k3, k4 = jax.random.split(key, 4)
        x = jax.random.normal(k1, (N, T, D), dtype=jnp.float32)
        h0 = jax.random.normal(k2, (N, H), dtype=jnp.float32)
        Wx = jax.random.normal(k3, (D, H), dtype=jnp.float32) / jnp.sqrt(jnp.float32(D))
        Wh = jax.random.normal(k4, (H, H), dtype=jnp.float32) / jnp.sqrt(jnp.float32(H))
        b = jnp.zeros((H,), dtype=jnp.float32)
        return {'x': x, 'h0': h0, 'Wx': Wx, 'Wh': Wh, 'b': b}
    _L1_cond_all = _L1_cond_setup()
    _L1_cond_in = {k: v for k, v in _L1_cond_all.items() if k in ('Wx', 'Wh', 'b')}
    del _L1_cond_all
    return {'x': x, 'cond_1024': cond_1024, 'L0_cond_weight': _L0_cond_in['weight'], 'L1_cond_Wx': _L1_cond_in['Wx'], 'L1_cond_Wh': _L1_cond_in['Wh'], 'L1_cond_b': _L1_cond_in['b']}

def reference(x, cond_1024, L0_cond_weight, L1_cond_Wx, L1_cond_Wh, L1_cond_b):
    import jax
    import jax.numpy as jnp

    def _L0_cond_ref(Efou, y, weight):
        import jax, jax.numpy as jnp
        import numpy as np
        IN_FEATURES = 512
        OUT_FEATURES = 512
        BATCH = 32
        SEQ = 512
        EPS = 1e-08
        scale = 1.0 / np.sqrt(np.float32(weight.shape[0]))
        ys = y * scale
        d = jax.lax.rsqrt(jnp.einsum('bi,io->bo', ys * ys, weight * weight) + EPS)
        out = jnp.einsum('bsi,io->bso', Efou * ys[:, None, :], weight) * d[:, None, :]
        return out

    def _L1_cond_ref(x, h0, Wx, Wh, b):
        import jax, jax.numpy as jnp
        import numpy as np
        N, T, D, H = (64, 256, 512, 512)
        xw = jnp.einsum('ntd,dh->nth', x, Wx) + b

        def step(prev_h, xw_t):
            next_h = jnp.tanh(xw_t + prev_h @ Wh)
            return (next_h, next_h)
        _, hs = jax.lax.scan(step, h0, jnp.swapaxes(xw, 0, 1))
        return jnp.swapaxes(hs, 0, 1)
    x = x + _L0_cond_ref(x, cond_1024, L0_cond_weight)
    x = x + _L1_cond_ref(x, cond_1024, L1_cond_Wx, L1_cond_Wh, L1_cond_b)
    return x

_drawn_inputs = setup_inputs


def setup_inputs(seed=0):
    import zlib

    import numpy as np

    out = dict(_drawn_inputs(seed))
    spreads = {'L1_cond_b': (0.0, 0.1)}
    factors = {}
    for name, (base, spread) in spreads.items():
        noise = np.random.default_rng([zlib.crc32(name.encode()), seed]).standard_normal(out[name].shape)
        drawn = base * np.exp(spread * noise) if base else spread * noise
        out[name] = jnp.asarray(drawn.astype(out[name].dtype))
    for name, factor in factors.items():
        out[name] = (out[name] * factor).astype(out[name].dtype)
    return out
```

```python
from contextlib import ExitStack

import concourse.bass as bass
from concourse import mybir

F32 = mybir.dt.float32
F32R = mybir.dt.float32r
ALU = mybir.AluOpType
ACT = mybir.ActivationFunctionType

G = 32
NJ = 4
NC = 4
STEPS = 16
QT = 4
NQ = STEPS // QT
DMA = 16
EPS = 1e-8


def build(nc, x, cond, w0, wx, wh, bias, out):
    B, SEQ, D = x.shape
    assert B == G and D == NJ * 128 and SEQ % (2 * STEPS) == 0
    NB = SEQ // STEPS
    COLS = STEPS * B
    HALF = B * QT
    SCALE = 1.0 / float(D) ** 0.5

    x_rows = x.rearrange("b t (j c) -> j b t c", j=NJ)
    out_rows = out.rearrange("b t (j c) -> j b t c", j=NJ)
    cond_rows = cond.rearrange("b (j c) -> j b c", j=NJ)

    def weight_rows(w):
        return w.rearrange("(j k p) n -> j p k n", j=NJ, k=NC)

    with ExitStack() as ctx:
        def sb(name, shape, dt=F32):
            return ctx.enter_context(nc.sbuf_tensor(name, shape, dt))

        def bank(name):
            return ctx.enter_context(nc.psum_tensor(name, [128, 512], F32))

        def sem(name):
            return ctx.enter_context(nc.semaphore(name))

        w0_hi = sb("w0_hi", [128, NC, NC, 128], F32R)
        w0_lo = sb("w0_lo", [128, NC, NC, 128], F32R)
        wx_hi = sb("wx_hi", [128, NC, NC, 128], F32R)
        wx_lo = sb("wx_lo", [128, NC, NC, 128], F32R)
        wh_sb = sb("wh_sb", [128, NC, D])
        cond_r = sb("cond_r", [128, 128])
        ys = sb("ys", [128, NC, B])
        ys2 = sb("ys2", [128, NC, B])
        dem = sb("dem", [128, NC, B])
        dem_s = sb("dem_s", [128, NC * B])
        dem_0 = sb("dem_0", [128, NC * B])
        dem_q = sb("dem_q", [128, NC * B])
        bias_r = sb("bias_r", [128, 128])
        bias_t = sb("bias_t", [128, NC, G])
        x_in = sb("x_in", [128, 2, STEPS, 128])
        x_t = sb("x_t", [128, 2, NC, STEPS, B])
        xs = sb("xs", [128, 2, STEPS, B])
        xs_hi = sb("xs_hi", [128, NC, COLS], F32R)
        xs_lo = sb("xs_lo", [128, NC, COLS], F32R)
        yd = sb("yd", [128, 2, STEPS, B])
        x1_t = sb("x1_t", [128, 2, NC, STEPS, B])
        x1_hi = sb("x1_hi", [128, NC, COLS], F32R)
        x1_lo = sb("x1_lo", [128, NC, COLS], F32R)
        xwb_t = sb("xwb_t", [128, 2, COLS])
        xwb = sb("xwb", [128, 2, STEPS, 128])
        h_r = sb("h_r", [128, 2, 128])
        h_t = sb("h_t", [128, STEPS, NC, B])
        o_t = sb("o_t", [128, 2, QT * 128])
        o_r = sb("o_r", [128, NQ, QT, 128])

        w0_raw = x1_t[:, 1].rearrange("p k t b -> p k (t b)")
        wx_raw = xwb[:, 0].rearrange("p (k t) c -> p k (t c)", k=NC)
        w0_sq = xwb[:, 1].rearrange("p (k c t) q -> p k c (t q)", k=NC, c=NC)

        z = [bank(f"z{i}") for i in range(2)]
        y_ps = [bank(f"y_ps{i}") for i in range(2)]
        xw_ps = [bank(f"xw_ps{i}") for i in range(4)]

        cond_in = sem("cond_in")
        bias_in = sem("bias_in")
        w0_in = sem("w0_in")
        wx_in = sem("wx_in")
        wh_in = sem("wh_in")
        bias_clear = sem("bias_clear")
        cond_turned = sem("cond_turned")
        ys_done = sem("ys_done")
        dem_step = sem("dem_step")
        w0_squared = sem("w0_squared")
        dem_summed = sem("dem_summed")
        dem_root = sem("dem_root")
        w0_hi_done = sem("w0_hi_done")
        w0_lo_done = sem("w0_lo_done")
        wx_hi_done = sem("wx_hi_done")
        wx_lo_done = sem("wx_lo_done")
        bias_done = sem("bias_done")
        x_loaded = [sem(f"x_loaded{i}") for i in range(2)]
        x_turned = sem("x_turned")
        xs_scaled = sem("xs_scaled")
        xs_hi_done = sem("xs_hi_done")
        xs_lo_done = sem("xs_lo_done")
        y_done = sem("y_done")
        yd_done = sem("yd_done")
        x1_done = sem("x1_done")
        x1_hi_done = sem("x1_hi_done")
        x1_lo_done = sem("x1_lo_done")
        xw_done = sem("xw_done")
        xwb_done = sem("xwb_done")
        xwb_turned = sem("xwb_turned")
        z_product = sem("z_product")
        z_summed = sem("z_summed")
        h_done = sem("h_done")
        h_turned = sem("h_turned")
        o_summed = sem("o_summed")
        o_turned = sem("o_turned")
        o_stored = [sem(f"o_stored{q}") for q in range(NQ)]

        def blk(n, k=0):
            return (n[0], n[1] + k)

        def par(n):
            return n[1] % 2

        def upto(rate, n, c):
            return 2 * rate * n[0] + (rate * n[1] + c)

        def pairs(n):
            return n[0] + n[1] // 2

        def exists(n):
            return not isinstance(n[0], int) or 0 <= 2 * n[0] + n[1] < NB

        def wait(eng, semaphore, count):
            if not isinstance(count, int) or count > 0:
                eng.wait_ge(semaphore, count)

        def schedule(eng, window, first=-2, tail=2):
            for n in range(first, 2):
                window((0, n))
            with eng.Fori(1, (NB - tail) // 2) as i:
                for k in range(2):
                    window((i, k))
            for n in range(NB - tail, NB):
                window((0, n))

        block = ctx.enter_context(nc.Block())

        @block.sync
        def _(sp):
            def load(m):
                if not exists(m):
                    return
                wait(sp, x_turned, upto(NQ, m, -NQ))
                start = 2 * STEPS * m[0] + STEPS * m[1]
                for j in range(NJ):
                    sp.dma_start(x_in[G * j:G * j + G, par(m)],
                                 x_rows[j][:, bass.ds(start, STEPS), :]).then_inc(x_loaded[par(m)], DMA)

            def store(m, q):
                if not exists(m):
                    return
                wait(sp, o_turned, upto(NQ, m, q + 1))
                start = 2 * STEPS * m[0] + (STEPS * m[1] + QT * q)
                for j in range(NJ):
                    sp.dma_start(out_rows[j][:, bass.ds(start, QT), :],
                                 o_r[G * j:G * j + G, q]).then_inc(o_stored[q], DMA)

            for j in range(NJ):
                sp.dma_start(cond_r[G * j:G * j + G, :], cond_rows[j]).then_inc(cond_in, DMA)
            load((0, 0))
            for j in range(NJ):
                sp.dma_start(wx_raw[G * j:G * j + G], weight_rows(wx)[j]).then_inc(wx_in, DMA)

            def window(n):
                load(blk(n, 3))
                store(blk(n, -1), NQ - 1)
                for q in range(NQ - 1):
                    store(n, q)

            schedule(sp, window, tail=4)
            store((0, NB - 1), NQ - 1)
            for q in range(NQ):
                sp.wait_ge(o_stored[q], NJ * DMA * NB)

        @block.scalar
        def _(act):
            for j in range(NJ):
                act.dma_start(w0_raw[G * j:G * j + G], weight_rows(w0)[j]).then_inc(w0_in, DMA)
            act.wait_ge(bias_clear, 1)
            act.dma_start(bias_r[0:128:G, :], bias.rearrange("(j c) -> j c", j=NJ)).then_inc(bias_in, DMA)
            for j in range(NJ):
                act.dma_start(wh_sb[G * j:G * j + G], weight_rows(wh)[j]).then_inc(wh_in, DMA)

            def split_weight(raw, hi, done):
                for k in range(NC):
                    nc.scalar.activation(hi[:, k].rearrange("p c (j i) -> p c j i", j=NJ),
                                         raw[:, k].rearrange("p (j c i) -> p c j i", j=NJ, c=NC),
                                         ACT.Copy).then_inc(done, 1)

            act.wait_ge(w0_in, NJ * DMA)
            split_weight(w0_raw, w0_hi, w0_hi_done)
            act.wait_ge(dem_step, 1)
            nc.scalar.activation(dem_0[:, :], dem_s[:, :], ACT.Sqrt).then_inc(dem_root, 1)
            act.wait_ge(wx_in, NJ * DMA)
            split_weight(wx_raw, wx_hi, wx_hi_done)

            def tanh(n, t):
                act.wait_ge(z_summed, upto(STEPS, n, t + 1))
                nc.scalar.activation(h_r[:, t % 2], z[t % 2][:, 0:128], ACT.Tanh).then_inc(h_done, 1)

            def xs_high(m, c):
                act.wait_ge(xs_scaled, upto(NC, m, c + 1))
                if c == 0:
                    wait(act, y_done, upto(NC, m, 0))
                nc.scalar.activation(xs_hi[:, c], xs[:, c % 2].rearrange("p t b -> p (t b)"),
                                     ACT.Copy).then_inc(xs_hi_done, 1)

            def x1_high(m, c):
                act.wait_ge(x1_done, upto(NC, m, c + 1))
                if c == 0:
                    wait(act, xw_done, upto(NC, m, 0))
                nc.scalar.activation(x1_hi[:, c], x1_t[:, par(m), c].rearrange("p t b -> p (t b)"),
                                     ACT.Copy).then_inc(x1_hi_done, 1)

            def add_bias(m, c):
                act.wait_ge(xw_done, upto(NC, m, c + 1))
                wait(act, xwb_turned, upto(NC, m, c - 1))
                nc.scalar.activation(xwb_t[:, c % 2], xw_ps[c][:, :], ACT.Identity,
                                     bias=bias_t[:, c, 0:1]).then_inc(xwb_done, 1)

            def window(n):
                ahead, next_ = blk(n, 2), blk(n, 1)
                fills = {1: [(x1_high, next_, 0)], 3: [(x1_high, next_, 1)], 5: [(x1_high, next_, 2)],
                         7: [(x1_high, next_, 3)], 9: [(xs_high, ahead, 0)],
                         10: [(add_bias, next_, 0), (xs_high, ahead, 1)],
                         11: [(add_bias, next_, 1), (xs_high, ahead, 2)],
                         12: [(add_bias, next_, 2), (xs_high, ahead, 3)],
                         14: [(add_bias, next_, 3)]}
                for t in range(STEPS):
                    if exists(n):
                        tanh(n, t)
                    for what, m, c in fills.get(t, []):
                        if exists(m):
                            what(m, c)

            act.wait_ge(bias_done, 1)
            schedule(act, window)

        @block.gpsimd
        def _(pool):
            def scale_x(m, c):
                if c == 0:
                    pool.wait_ge(x_turned, upto(NQ, m, NQ))
                wait(pool, xs_lo_done, upto(NC, m, c - 1))
                nc.gpsimd.tensor_tensor(xs[:, c % 2], x_t[:, par(m), c],
                                        ys[:, c:c + 1, :].broadcast_to([128, STEPS, B]), ALU.mult).then_inc(xs_scaled, 1)

            def xs_low(m, c):
                pool.wait_ge(xs_hi_done, upto(NC, m, c + 1))
                nc.gpsimd.tensor_tensor(xs_lo[:, c], xs[:, c % 2].rearrange("p t b -> p (t b)"),
                                        xs_hi[:, c].bitcast(F32), ALU.subtract).then_inc(xs_lo_done, 1)

            def sum_x1(m, c):
                pool.wait_ge(yd_done, upto(NC, m, c + 1))
                if c == 0:
                    wait(pool, o_summed, upto(NQ, m, -NQ))
                nc.gpsimd.tensor_tensor(x1_t[:, par(m), c], yd[:, c % 2], x_t[:, par(m), c],
                                        ALU.add).then_inc(x1_done, 1)

            def x1_low(m, c):
                pool.wait_ge(x1_hi_done, upto(NC, m, c + 1))
                nc.gpsimd.tensor_tensor(x1_lo[:, c], x1_t[:, par(m), c].rearrange("p t b -> p (t b)"),
                                        x1_hi[:, c].bitcast(F32), ALU.subtract).then_inc(x1_lo_done, 1)

            def sum_out(m, q):
                pool.wait_ge(h_turned, upto(STEPS, m, QT * q + QT + 1))
                wait(pool, o_turned, upto(NQ, m, q - 1))
                nc.gpsimd.tensor_tensor(
                    o_t[:, q % 2].rearrange("p (t c b) -> p c t b", t=QT, c=NC),
                    h_t[:, QT * q:QT * q + QT].rearrange("p t c b -> p c t b"),
                    x1_t[:, par(m), :, QT * q:QT * q + QT, :], ALU.add).then_inc(o_summed, 1)

            def window(n):
                ahead, next_, last = blk(n, 2), blk(n, 1), blk(n, -1)
                order = [(sum_out, last, 3), (sum_x1, next_, 0), (x1_low, next_, 0), (sum_x1, next_, 1),
                         (x1_low, next_, 1), (sum_out, n, 0), (sum_x1, next_, 2), (x1_low, next_, 2),
                         (sum_x1, next_, 3), (x1_low, next_, 3), (scale_x, ahead, 0), (scale_x, ahead, 1),
                         (sum_out, n, 1), (xs_low, ahead, 0), (scale_x, ahead, 2), (xs_low, ahead, 1),
                         (scale_x, ahead, 3), (xs_low, ahead, 2), (xs_low, ahead, 3), (sum_out, n, 2)]
                for what, m, c in order:
                    if exists(m):
                        what(m, c)

            pool.wait_ge(ys_done, 1)
            schedule(pool, window)
            sum_out((0, NB - 1), NQ - 1)

        @block.vector
        def _(dve):
            def turn_x(m, q):
                if q == 0:
                    dve.wait_ge(x_loaded[par(m)], 1 * (NJ * DMA * (pairs(m) + 1)))
                    wait(dve, x1_done, upto(NC, m, -NC))
                nc.vector.transpose(
                    x_t[:, par(m), :, QT * q:QT * q + QT, :].rearrange("p c t b -> p t c b"),
                    x_in[:, par(m), QT * q:QT * q + QT, :]).then_inc(x_turned, 1)

            def scale_y(m, c):
                dve.wait_ge(y_done, upto(NC, m, c + 1))
                wait(dve, x1_done, upto(NC, m, c - 1))
                nc.vector.tensor_tensor(yd[:, c % 2], y_ps[c % 2][:, :].rearrange("p (t b) -> p t b", b=B),
                                        dem[:, c:c + 1, :].broadcast_to([128, STEPS, B]), ALU.mult).then_inc(yd_done, 1)

            def turn_xwb(m, c):
                dve.wait_ge(xwb_done, upto(NC, m, c + 1))
                nc.vector.transpose(xwb[:, par(m), :, G * c:G * c + G],
                                    xwb_t[:, c % 2].rearrange("p (t b) -> p t b", b=B)).then_inc(xwb_turned, 1)

            def turn_out(m, q):
                dve.wait_ge(o_summed, upto(NQ, m, q + 1))
                wait(dve, o_stored[q], upto(NJ * DMA, m, 0))
                nc.vector.transpose(o_r[:, q].rearrange("p t c -> p (t c)"),
                                    o_t[:, q % 2]).then_inc(o_turned, 1)

            def chain(n, t):
                dve.wait_ge(z_product, upto(STEPS, n, t + 1))
                if t == 0:
                    dve.wait_ge(xwb_turned, upto(NC, n, NC))
                nc.vector.tensor_tensor(z[t % 2][:, 0:128], z[t % 2][:, 0:128], xwb[:, par(n), t],
                                        ALU.add).then_inc(z_summed, 1)
                dve.wait_ge(h_done, upto(STEPS, n, t + 1))
                if t % QT == 0:
                    wait(dve, o_summed, upto(NQ, n, t // QT + 1 - NQ))
                nc.vector.transpose(h_t[:, t].rearrange("p c b -> p (c b)"), h_r[:, t % 2]).then_inc(h_turned, 1)

            def window(n):
                ahead, next_, last = blk(n, 2), blk(n, 1), blk(n, -1)
                fills = {0: (scale_y, next_, 0), 2: (scale_y, next_, 1), 4: (scale_y, next_, 2),
                         6: (scale_y, next_, 3), 1: (turn_x, ahead, 0), 3: (turn_x, ahead, 1),
                         5: (turn_x, ahead, 2), 7: (turn_x, ahead, 3), 10: (turn_xwb, next_, 0),
                         11: (turn_xwb, next_, 1), 13: (turn_xwb, next_, 2), 15: (turn_xwb, next_, 3),
                         8: (turn_out, last, 3), 9: (turn_out, n, 0), 12: (turn_out, n, 1),
                         14: (turn_out, n, 2)}
                for t in range(STEPS):
                    if exists(n):
                        chain(n, t)
                    what, m, c = fills[t]
                    if exists(m):
                        what(m, c)

            nc.vector.memset(bias_r[:, :], 0.0).then_inc(bias_clear, 1)
            dve.wait_ge(cond_in, NJ * DMA)
            h_start = h_t[:, STEPS - 1].rearrange("p c b -> p (c b)")
            nc.vector.transpose(h_start, cond_r[:, :]).then_inc(h_turned, 1)
            dve.wait_ge(h_turned, 1)
            ys_flat = ys[:, :, :].rearrange("p c b -> p (c b)")
            nc.vector.tensor_scalar(ys_flat, h_start, SCALE, None, ALU.mult).then_inc(ys_done, 1)
            dve.wait_ge(ys_done, 1)
            nc.vector.tensor_tensor(ys2[:, :, :], ys[:, :, :], ys[:, :, :], ALU.mult).then_inc(ys_done, 1)
            dve.wait_ge(w0_in, NJ * DMA)
            for k in range(NC):
                raw = w0_raw[:, k].rearrange("p (j c i) -> p c j i", j=NJ, c=NC)
                nc.vector.tensor_tensor(w0_sq[:, k].rearrange("p c (j i) -> p c j i", j=NJ), raw, raw,
                                        ALU.mult).then_inc(w0_squared, 1)

            def weight_low(raw, hi, lo, hi_done, lo_done):
                for k in range(NC):
                    dve.wait_ge(hi_done, k + 1)
                    nc.vector.tensor_tensor(lo[:, k].rearrange("p c (j i) -> p c j i", j=NJ),
                                            raw[:, k].rearrange("p (j c i) -> p c j i", j=NJ, c=NC),
                                            hi[:, k].bitcast(F32).rearrange("p c (j i) -> p c j i", j=NJ),
                                            ALU.subtract).then_inc(lo_done, 1)

            weight_low(w0_raw, w0_hi, w0_lo, w0_hi_done, w0_lo_done)
            dve.wait_ge(bias_in, DMA)
            nc.vector.transpose(bias_t[:, :, :].rearrange("p c b -> p (c b)"), bias_r[:, :]).then_inc(bias_done, 1)
            dve.wait_ge(dem_summed, 1)
            nc.vector.tensor_scalar(dem_s[:, :], y_ps[1][:, 0:NC * B], EPS, None, ALU.add).then_inc(dem_step, 1)
            dve.wait_ge(dem_root, 1)
            nc.vector.reciprocal(dem_0[:, :], dem_0[:, :]).then_inc(dem_step, 1)
            dve.wait_ge(dem_step, 2)
            nc.vector.tensor_tensor(dem_q[:, :], dem_0[:, :], dem_0[:, :], ALU.mult).then_inc(dem_step, 1)
            dve.wait_ge(dem_step, 3)
            nc.vector.tensor_tensor(dem_q[:, :], dem_q[:, :], dem_s[:, :], ALU.mult).then_inc(dem_step, 1)
            dve.wait_ge(dem_step, 4)
            nc.vector.tensor_scalar(dem_q[:, :], dem_q[:, :], -0.5, 1.5, ALU.mult, ALU.add).then_inc(dem_step, 1)
            dve.wait_ge(dem_step, 5)
            nc.vector.tensor_tensor(dem[:, :, :].rearrange("p c b -> p (c b)"), dem_0[:, :], dem_q[:, :],
                                    ALU.mult).then_inc(dem_step, 1)
            dve.wait_ge(dem_step, 6)
            weight_low(wx_raw, wx_hi, wx_lo, wx_hi_done, wx_lo_done)
            schedule(dve, window)
            turn_out((0, NB - 1), NQ - 1)

        @block.tensor
        def _(pe):
            def passes(ps, w_hi, w_lo, a_hi, a_lo, k, c, first, last):
                yield ps[:, :], w_lo[:, k, c], a_hi[:, k], first, False
                yield ps[:, :], w_hi[:, k, c], a_lo[:, k], False, False
                yield ps[:, :], w_hi[:, k, c], a_hi[:, k], False, last

            def dense(m, w_hi, w_lo, a_hi, a_lo, banks, c, k):
                n_banks = len(banks)
                for args in passes(banks[c % n_banks], w_hi, w_lo, a_hi, a_lo, k, c, k == 0, k == NC - 1):
                    yield args

            def y_chunk(m, c):
                wait(pe, yd_done, upto(NC, m, c - 1))
                for k in range(NC):
                    if c == 0:
                        pe.wait_ge(xs_lo_done, upto(NC, m, k + 1))
                    for ps, w, a, first, last in dense(m, w0_hi, w0_lo, xs_hi, xs_lo, y_ps, c, k):
                        mm = nc.tensor.matmul(ps, w, a, start=first, stop=last)
                        if last:
                            mm.then_inc(y_done, 1)
                        yield

            def xw_chunks(m, parts):
                for c, k in parts:
                    if c == 0:
                        pe.wait_ge(x1_lo_done, upto(NC, m, k + 1))
                    if k == 0:
                        wait(pe, xwb_done, upto(NC, m, c - 3))
                    for ps, w, a, first, last in dense(m, wx_hi, wx_lo, x1_hi, x1_lo, xw_ps, c, k):
                        mm = nc.tensor.matmul(ps, w, a, start=first, stop=last)
                        if last:
                            mm.then_inc(xw_done, 1)
                        yield

            def chain(n, t):
                pe.wait_ge(h_turned, upto(STEPS, n, t + 1))
                for k in range(NC):
                    for j in range(NJ):
                        mm = nc.tensor.matmul(z[t % 2][G * j:G * j + G, 0:128], h_t[:, (t - 1) % STEPS, k],
                                              wh_sb[:, k, 128 * j:128 * j + 128], start=(k == 0), stop=(k == NC - 1))
                mm.then_inc(z_product, 1)

            XW_PARTS = [(0, 0), (0, 1), (1, 0), (1, 1), (0, 2), (1, 2), (0, 3), (1, 3)] + \
                       [(c, k) for c in (2, 3) for k in range(NC)]

            def fill(n):
                ahead, next_ = blk(n, 2), blk(n, 1)
                if exists(next_):
                    for c in range(1, NC):
                        yield from y_chunk(next_, c)
                    yield from xw_chunks(next_, XW_PARTS)
                if exists(ahead):
                    yield from y_chunk(ahead, 0)

            def window(n):
                products = fill(n)
                for t in range(STEPS):
                    if exists(n):
                        chain(n, t)
                    for _ in range(2 * 3 * NC * NC // STEPS):
                        next(products, None)
                for _ in products:
                    pass

            pe.wait_ge(ys_done, 2)
            pe.wait_ge(w0_squared, NC)
            for c in range(NC):
                for k in range(NC):
                    mm = nc.tensor.matmul(y_ps[1][:, B * c:B * c + B], w0_sq[:, k, c], ys2[:, k],
                                          start=(k == 0), stop=(k == NC - 1))
            mm.then_inc(dem_summed, 1)
            pe.wait_ge(w0_lo_done, NC)
            for _ in y_chunk((0, 0), 0):
                pass
            pe.wait_ge(wh_in, NJ * DMA)
            pe.wait_ge(wx_lo_done, NC)
            schedule(pe, window, first=-1)


_INS = ['x', 'cond_1024', 'L0_cond_weight', 'L1_cond_Wx', 'L1_cond_Wh', 'L1_cond_b']
_OUTS = [((32, 512, 512), 'float32')]


def kernel(**inputs):
    import numpy as _np
    import concourse.bacc as _bacc
    from concourse import mybir as _mybir
    from concourse.bass_utils import run_bass_kernel_spmd as _run

    nc = _bacc.Bacc("TRN2", target_bir_lowering=False, num_devices=1)
    arrays, args = {}, []
    for name in _INS:
        a = _np.ascontiguousarray(inputs[name])
        arrays[f"in_{name}_dram"] = a
        args.append(nc.dram_tensor(f"in_{name}_dram", a.shape, _mybir.dt.from_np(a.dtype), kind="ExternalInput").ap())
    for i, (shape, dtype) in enumerate(_OUTS):
        dt = _mybir.dt.from_np(_np.dtype(dtype))
        args.append(nc.dram_tensor(f"out_{i}_dram", shape, dt, kind="ExternalOutput").ap())
    build(nc, *args)
    r = _run(nc, [arrays], core_ids=[0])
    return r.results[0]["out_0_dram"]
```

```python
from contextlib import ExitStack

import concourse.bass as bass
from concourse import mybir

F32 = mybir.dt.float32
F32R = mybir.dt.float32r
ALU = mybir.AluOpType
ACT = mybir.ActivationFunctionType

G = 32
NJ = 4
NC = 4
STEPS = 16
QT = 4
NQ = STEPS // QT
DMA = 16
EPS = 1e-8


def build(nc, x, cond, w0, wx, wh, bias, out):
    B, SEQ, D = x.shape
    assert B == G and D == NJ * 128 and SEQ % (2 * STEPS) == 0
    NB = SEQ // STEPS
    COLS = STEPS * B
    SCALE = 1.0 / float(D) ** 0.5

    x_rows = x.rearrange("b t (j c) -> j b t c", j=NJ)
    out_rows = out.rearrange("b t (j c) -> j b t c", j=NJ)
    cond_rows = cond.rearrange("b (j c) -> j b c", j=NJ)

    def weight_rows(w):
        return w.rearrange("(j k p) n -> j p k n", j=NJ, k=NC)

    with ExitStack() as ctx:
        def sb(name, shape, dt=F32):
            return ctx.enter_context(nc.sbuf_tensor(name, shape, dt))

        def bank(name):
            return ctx.enter_context(nc.psum_tensor(name, [128, 512], F32))

        def sem(name):
            return ctx.enter_context(nc.semaphore(name))

        w0_hi = sb("w0_hi", [128, NC, NC, 128], F32R)
        w0_lo = sb("w0_lo", [128, NC, NC, 128], F32R)
        wx_hi = sb("wx_hi", [128, NC, NC, 128], F32R)
        wx_lo = sb("wx_lo", [128, NC, NC, 128], F32R)
        wh_sb = sb("wh_sb", [128, NC, D])
        cond_r = sb("cond_r", [128, 128])
        ys = sb("ys", [128, NC, B])
        ys2 = sb("ys2", [128, NC, B])
        dem = sb("dem", [128, NC, B])
        dem_s = sb("dem_s", [128, 128])
        dem_0 = sb("dem_0", [128, 128])
        dem_q = sb("dem_q", [128, 128])
        table_probe = sb("table_probe", [128, 2])
        bias_r = sb("bias_r", [128, 128])
        bias_t = sb("bias_t", [128, NC, G])
        x_in = sb("x_in", [128, 2, STEPS, 128])
        x_t = sb("x_t", [128, 2, NC, STEPS, B])
        xs = sb("xs", [128, 2, STEPS, B])
        xs_hi = sb("xs_hi", [128, NC, COLS], F32R)
        xs_lo = sb("xs_lo", [128, NC, COLS], F32R)
        yd = sb("yd", [128, 2, STEPS, B])
        x1_t = sb("x1_t", [128, 2, NC, STEPS, B])
        x1_hi = sb("x1_hi", [128, NC, COLS], F32R)
        x1_lo = sb("x1_lo", [128, NC, COLS], F32R)
        xwb_t = sb("xwb_t", [128, 2, COLS])
        xwb = sb("xwb", [128, 2, STEPS, 128])
        h_r = sb("h_r", [128, 2, 128])
        h_t = sb("h_t", [128, STEPS, NC, B])
        o_t = sb("o_t", [128, 2, QT * 128])
        o_r = sb("o_r", [128, NQ, QT, 128])

        w0_raw = x1_t[:, 1].rearrange("p k t b -> p k (t b)")
        wx_raw = xwb[:, 0].rearrange("p (k t) c -> p k (t c)", k=NC)
        w0_sq = xwb[:, 1].rearrange("p (k t) c -> p k (t c)", k=NC)

        z = [bank(f"z{i}") for i in range(2)]
        y_ps = [bank(f"y_ps{i}") for i in range(2)]
        xw_ps = [bank(f"xw_ps{i}") for i in range(4)]

        cond_in = sem("cond_in")
        bias_in = sem("bias_in")
        w0_in = sem("w0_in")
        wx_in = sem("wx_in")
        wh_in = sem("wh_in")
        bias_clear = sem("bias_clear")
        probe_clear = sem("probe_clear")
        probe_rooted = sem("probe_rooted")
        cond_turned = sem("cond_turned")
        ys_done = sem("ys_done")
        dem_step = sem("dem_step")
        w0_squared = sem("w0_squared")
        dem_summed = sem("dem_summed")
        dem_root = sem("dem_root")
        w0_hi_done = sem("w0_hi_done")
        w0_lo_done = sem("w0_lo_done")
        wx_hi_done = sem("wx_hi_done")
        wx_lo_done = sem("wx_lo_done")
        bias_done = sem("bias_done")
        x_loaded = [sem(f"x_loaded{i}") for i in range(2)]
        x_turned = sem("x_turned")
        xs_scaled = sem("xs_scaled")
        xs_hi_done = sem("xs_hi_done")
        xs_lo_done = sem("xs_lo_done")
        y_done = sem("y_done")
        yd_done = sem("yd_done")
        x1_done = sem("x1_done")
        x1_hi_done = sem("x1_hi_done")
        x1_lo_done = sem("x1_lo_done")
        xw_done = sem("xw_done")
        xwb_done = sem("xwb_done")
        xwb_turned = sem("xwb_turned")
        z_product = sem("z_product")
        z_summed = sem("z_summed")
        h_done = sem("h_done")
        h_turned = sem("h_turned")
        o_summed = sem("o_summed")
        o_turned = sem("o_turned")
        o_stored = [sem(f"o_stored{q}") for q in range(NQ)]

        def blk(n, k=0):
            return (n[0], n[1] + k)

        def par(n):
            return n[1] % 2

        def upto(rate, n, c):
            return 2 * rate * n[0] + (rate * n[1] + c)

        def pairs(n):
            return n[0] + n[1] // 2

        def exists(n):
            return not isinstance(n[0], int) or 0 <= 2 * n[0] + n[1] < NB

        def is_block_0(n):
            return isinstance(n[0], int) and 2 * n[0] + n[1] == 0

        def y_bank(m, c):
            return xw_ps[c] if is_block_0(m) and c >= 2 else y_ps[c % 2]

        def is_early(m, what):
            if what in (scale_x, xs_low):
                return is_block_0(m) or is_block_0(blk(m, -1))
            return what in (sum_x1, x1_low) and is_block_0(m)

        def wait(eng, semaphore, count):
            if not isinstance(count, int) or count > 0:
                eng.wait_ge(semaphore, count)

        def schedule(eng, window, first=-2, tail=2):
            for n in range(first, 2):
                window((0, n))
            with eng.Fori(1, (NB - tail) // 2) as i:
                for k in range(2):
                    window((i, k))
            for n in range(NB - tail, NB):
                window((0, n))

        def scale_x(eng, m, c):
            if c == 0:
                eng.wait_ge(x_turned, upto(NQ, m, NQ))
            wait(eng, xs_lo_done, upto(NC, m, c - 1))
            eng.tensor_tensor(xs[:, c % 2], x_t[:, par(m), c],
                              ys[:, c:c + 1, :].broadcast_to([128, STEPS, B]), ALU.mult).then_inc(xs_scaled, 1)

        def xs_low(eng, m, c):
            eng.wait_ge(xs_hi_done, upto(NC, m, c + 1))
            eng.tensor_tensor(xs_lo[:, c], xs[:, c % 2].rearrange("p t b -> p (t b)"),
                              xs_hi[:, c].bitcast(F32), ALU.subtract).then_inc(xs_lo_done, 1)

        def sum_x1(eng, m, c):
            eng.wait_ge(yd_done, upto(NC, m, c + 1))
            if c == 0:
                wait(eng, o_summed, upto(NQ, m, -NQ))
            eng.tensor_tensor(x1_t[:, par(m), c], yd[:, c % 2], x_t[:, par(m), c],
                              ALU.add).then_inc(x1_done, 1)

        def x1_low(eng, m, c):
            eng.wait_ge(x1_hi_done, upto(NC, m, c + 1))
            eng.tensor_tensor(x1_lo[:, c], x1_t[:, par(m), c].rearrange("p t b -> p (t b)"),
                              x1_hi[:, c].bitcast(F32), ALU.subtract).then_inc(x1_lo_done, 1)

        def weight_low(eng, k, raw, hi, lo, hi_done, lo_done):
            eng.wait_ge(hi_done, k + 1)
            eng.tensor_tensor(lo[:, k].rearrange("p c (j i) -> p c j i", j=NJ),
                              raw[:, k].rearrange("p (j c i) -> p c j i", j=NJ, c=NC),
                              hi[:, k].bitcast(F32).rearrange("p c (j i) -> p c j i", j=NJ),
                              ALU.subtract).then_inc(lo_done, 1)

        block = ctx.enter_context(nc.Block())

        @block.sync
        def _(sp):
            def load(m):
                if not exists(m):
                    return
                wait(sp, x_turned, upto(NQ, m, -NQ))
                start = 2 * STEPS * m[0] + STEPS * m[1]
                for j in range(NJ):
                    sp.dma_start(x_in[G * j:G * j + G, par(m)],
                                 x_rows[j][:, bass.ds(start, STEPS), :]).then_inc(x_loaded[par(m)], DMA)

            def store(m, q):
                if not exists(m):
                    return
                wait(sp, o_turned, upto(NQ, m, q + 1))
                start = 2 * STEPS * m[0] + (STEPS * m[1] + QT * q)
                for j in range(NJ):
                    sp.dma_start(out_rows[j][:, bass.ds(start, QT), :],
                                 o_r[G * j:G * j + G, q]).then_inc(o_stored[q], DMA)

            load((0, 0))
            for j in range(NJ):
                sp.dma_start(cond_r[G * j:G * j + G, :], cond_rows[j]).then_inc(cond_in, DMA)
            sp.wait_ge(x_loaded[0], NJ * DMA)
            for j in range(NJ):
                sp.dma_start(wx_raw[G * j:G * j + G], weight_rows(wx)[j]).then_inc(wx_in, DMA)
            sp.wait_ge(bias_clear, 1)
            sp.dma_start(bias_r[0:128:G, :], bias.rearrange("(j c) -> j c", j=NJ)).then_inc(bias_in, DMA)

            def window(n):
                load(blk(n, 3))
                if is_block_0(blk(n, 2)):
                    for j in range(NJ):
                        sp.dma_start(wh_sb[G * j:G * j + G], weight_rows(wh)[j]).then_inc(wh_in, DMA)
                store(blk(n, -1), NQ - 1)
                for q in range(NQ - 1):
                    store(n, q)

            schedule(sp, window, tail=4)
            store((0, NB - 1), NQ - 1)
            for q in range(NQ):
                sp.wait_ge(o_stored[q], NJ * DMA * NB)

        @block.scalar
        def _(act):
            act.wait_ge(probe_clear, 1)
            nc.scalar.activation(table_probe[:, 0:1], table_probe[:, 0:1], ACT.Sqrt).then_inc(probe_rooted, 1)
            for j in range(NJ):
                act.dma_start(w0_raw[G * j:G * j + G], weight_rows(w0)[j]).then_inc(w0_in, DMA)

            def split_weight(raw, hi, done):
                for k in range(NC):
                    nc.scalar.activation(hi[:, k].rearrange("p c (j i) -> p c j i", j=NJ),
                                         raw[:, k].rearrange("p (j c i) -> p c j i", j=NJ, c=NC),
                                         ACT.Copy).then_inc(done, 1)

            def tanh(n, t):
                act.wait_ge(z_summed, upto(STEPS, n, t + 1))
                nc.scalar.activation(h_r[:, t % 2], z[t % 2][:, 0:128], ACT.Tanh).then_inc(h_done, 1)

            def xs_high(m, c):
                act.wait_ge(xs_scaled, upto(NC, m, c + 1))
                if c == 0:
                    wait(act, y_done, upto(NC, m, 0))
                nc.scalar.activation(xs_hi[:, c], xs[:, c % 2].rearrange("p t b -> p (t b)"),
                                     ACT.Copy).then_inc(xs_hi_done, 1)

            def x1_high(m, c):
                act.wait_ge(x1_done, upto(NC, m, c + 1))
                if c == 0:
                    wait(act, xw_done, upto(NC, m, 0))
                nc.scalar.activation(x1_hi[:, c], x1_t[:, par(m), c].rearrange("p t b -> p (t b)"),
                                     ACT.Copy).then_inc(x1_hi_done, 1)

            def add_bias(m, c):
                act.wait_ge(xw_done, upto(NC, m, c + 1))
                wait(act, xwb_turned, upto(NC, m, c - 1))
                nc.scalar.activation(xwb_t[:, c % 2], xw_ps[c][:, :], ACT.Identity,
                                     bias=bias_t[:, c, 0:1]).then_inc(xwb_done, 1)

            def window(n):
                ahead, next_ = blk(n, 2), blk(n, 1)
                fills = {1: [(x1_high, next_, 0)], 3: [(x1_high, next_, 1)], 5: [(x1_high, next_, 2)],
                         7: [(x1_high, next_, 3)], 9: [(xs_high, ahead, 0)],
                         10: [(add_bias, next_, 0), (xs_high, ahead, 1)],
                         11: [(add_bias, next_, 1), (xs_high, ahead, 2)],
                         12: [(add_bias, next_, 2), (xs_high, ahead, 3)],
                         14: [(add_bias, next_, 3)]}
                for t in range(STEPS):
                    if exists(n):
                        tanh(n, t)
                    for what, m, c in fills.get(t, []):
                        if exists(m):
                            what(m, c)

            act.wait_ge(w0_in, NJ * DMA)
            split_weight(w0_raw, w0_hi, w0_hi_done)
            for k in range(NC):
                nc.scalar.activation(w0_sq[:, k], w0_raw[:, k], ACT.Square).then_inc(w0_squared, 1)
            for c in range(NC):
                xs_high((0, 0), c)
            act.wait_ge(wx_in, NJ * DMA)
            split_weight(wx_raw, wx_hi, wx_hi_done)
            act.wait_ge(dem_step, 1)
            nc.scalar.activation(dem_0[:, :], dem_s[:, :], ACT.Sqrt).then_inc(dem_root, 1)
            act.wait_ge(probe_rooted, 1)
            nc.scalar.activation(table_probe[:, 1:2], table_probe[:, 0:1], ACT.Tanh)
            act.wait_ge(bias_done, 1)
            schedule(act, window, first=-1)

        @block.gpsimd
        def _(pool):
            def sum_out(pool, m, q):
                pool.wait_ge(h_turned, upto(STEPS, m, QT * q + QT + 1))
                wait(pool, o_turned, upto(NQ, m, q - 1))
                nc.gpsimd.tensor_tensor(
                    o_t[:, q % 2].rearrange("p (t c b) -> p c t b", t=QT, c=NC),
                    h_t[:, QT * q:QT * q + QT].rearrange("p t c b -> p c t b"),
                    x1_t[:, par(m), :, QT * q:QT * q + QT, :], ALU.add).then_inc(o_summed, 1)

            def window(n):
                ahead, next_, last = blk(n, 2), blk(n, 1), blk(n, -1)
                order = [(sum_out, last, 3), (sum_x1, next_, 0), (x1_low, next_, 0), (sum_x1, next_, 1),
                         (x1_low, next_, 1), (sum_out, n, 0), (sum_x1, next_, 2), (x1_low, next_, 2),
                         (sum_x1, next_, 3), (x1_low, next_, 3), (scale_x, ahead, 0), (scale_x, ahead, 1),
                         (sum_out, n, 1), (xs_low, ahead, 0), (scale_x, ahead, 2), (xs_low, ahead, 1),
                         (scale_x, ahead, 3), (xs_low, ahead, 2), (xs_low, ahead, 3), (sum_out, n, 2)]
                for what, m, c in order:
                    if exists(m) and not is_early(m, what):
                        what(pool, m, c)

            for k in range(NC):
                weight_low(pool, k, w0_raw, w0_hi, w0_lo, w0_hi_done, w0_lo_done)
            for k in range(NC):
                weight_low(pool, k, wx_raw, wx_hi, wx_lo, wx_hi_done, wx_lo_done)
            pool.wait_ge(ys_done, 1)
            schedule(pool, window, first=-1)
            sum_out(pool, (0, NB - 1), NQ - 1)

        @block.vector
        def _(dve):
            def turn_x(m, q):
                if q == 0:
                    dve.wait_ge(x_loaded[par(m)], (pairs(m) + 1) * (NJ * DMA))
                    wait(dve, x1_done, upto(NC, m, -NC))
                nc.vector.transpose(
                    x_t[:, par(m), :, QT * q:QT * q + QT, :].rearrange("p c t b -> p t c b"),
                    x_in[:, par(m), QT * q:QT * q + QT, :]).then_inc(x_turned, 1)

            def scale_y(m, c):
                dve.wait_ge(y_done, upto(NC, m, c + 1))
                bank = y_bank(m, c)
                wait(dve, x1_done, upto(NC, m, c - 1))
                nc.vector.tensor_tensor(yd[:, c % 2], bank[:, :].rearrange("p (t b) -> p t b", b=B),
                                        dem[:, c:c + 1, :].broadcast_to([128, STEPS, B]), ALU.mult).then_inc(yd_done, 1)

            def turn_xwb(m, c):
                dve.wait_ge(xwb_done, upto(NC, m, c + 1))
                nc.vector.transpose(xwb[:, par(m), :, G * c:G * c + G],
                                    xwb_t[:, c % 2].rearrange("p (t b) -> p t b", b=B)).then_inc(xwb_turned, 1)

            def turn_out(m, q):
                dve.wait_ge(o_summed, upto(NQ, m, q + 1))
                wait(dve, o_stored[q], upto(NJ * DMA, m, 0))
                nc.vector.transpose(o_r[:, q].rearrange("p t c -> p (t c)"),
                                    o_t[:, q % 2]).then_inc(o_turned, 1)

            def chain(n, t):
                dve.wait_ge(z_product, upto(STEPS, n, t + 1))
                if t == 0:
                    dve.wait_ge(xwb_turned, upto(NC, n, NC))
                nc.vector.tensor_tensor(z[t % 2][:, 0:128], z[t % 2][:, 0:128], xwb[:, par(n), t],
                                        ALU.add).then_inc(z_summed, 1)
                dve.wait_ge(h_done, upto(STEPS, n, t + 1))
                if t % QT == 0:
                    wait(dve, o_summed, upto(NQ, n, t // QT + 1 - NQ))
                nc.vector.transpose(h_t[:, t].rearrange("p c b -> p (c b)"), h_r[:, t % 2]).then_inc(h_turned, 1)

            def window(n):
                ahead, next_, last = blk(n, 2), blk(n, 1), blk(n, -1)
                fills = {0: (scale_y, next_, 0), 2: (scale_y, next_, 1), 4: (scale_y, next_, 2),
                         6: (scale_y, next_, 3), 1: (turn_x, ahead, 0), 3: (turn_x, ahead, 1),
                         5: (turn_x, ahead, 2), 7: (turn_x, ahead, 3), 10: (turn_xwb, next_, 0),
                         11: (turn_xwb, next_, 1), 13: (turn_xwb, next_, 2), 15: (turn_xwb, next_, 3),
                         8: (turn_out, last, 3), 9: (turn_out, n, 0), 12: (turn_out, n, 1),
                         14: (turn_out, n, 2)}
                for t in range(STEPS):
                    if exists(n):
                        chain(n, t)
                    what, m, c = fills[t]
                    if exists(m):
                        what(m, c)

            nc.vector.memset(bias_r[:, :], 0.0).then_inc(bias_clear, 1)
            nc.vector.memset(table_probe[:, :], 0.0).then_inc(probe_clear, 1)
            dve.wait_ge(cond_in, NJ * DMA)
            h_start = h_t[:, STEPS - 1].rearrange("p c b -> p (c b)")
            nc.vector.transpose(h_start, cond_r[:, :]).then_inc(h_turned, 1)
            dve.wait_ge(h_turned, 1)
            ys_flat = ys[:, :, :].rearrange("p c b -> p (c b)")
            nc.vector.tensor_scalar(ys_flat, h_start, SCALE, None, ALU.mult).then_inc(ys_done, 1)
            dve.wait_ge(ys_done, 1)
            nc.vector.tensor_tensor(ys2[:, :, :], ys[:, :, :], ys[:, :, :], ALU.mult).then_inc(ys_done, 1)
            first, second = (0, 0), (0, 1)
            for q in range(NQ):
                turn_x(first, q)
            scale_x(dve, first, 0)
            scale_x(dve, first, 1)
            for c in range(NC):
                xs_low(dve, first, c)
                if c + 2 < NC:
                    scale_x(dve, first, c + 2)
            dve.wait_ge(bias_in, DMA)
            nc.vector.transpose(bias_t[:, :, :].rearrange("p c b -> p (c b)"), bias_r[:, :]).then_inc(bias_done, 1)
            dve.wait_ge(dem_summed, 1)
            nc.vector.tensor_scalar(dem_s[:, :], xw_ps[0][:, 0:128], EPS, None, ALU.add).then_inc(dem_step, 1)
            dve.wait_ge(dem_root, 1)
            nc.vector.reciprocal(dem_0[:, :], dem_0[:, :]).then_inc(dem_step, 1)
            dve.wait_ge(dem_step, 2)
            nc.vector.tensor_tensor(dem_q[:, :], dem_0[:, :], dem_0[:, :], ALU.mult).then_inc(dem_step, 1)
            dve.wait_ge(dem_step, 3)
            nc.vector.tensor_tensor(dem_q[:, :], dem_q[:, :], dem_s[:, :], ALU.mult).then_inc(dem_step, 1)
            dve.wait_ge(dem_step, 4)
            nc.vector.tensor_scalar(dem_q[:, :], dem_q[:, :], -0.5, 1.5, ALU.mult, ALU.add).then_inc(dem_step, 1)
            dve.wait_ge(dem_step, 5)
            nc.vector.tensor_tensor(dem_q[:, :], dem_0[:, :], dem_q[:, :], ALU.mult).then_inc(dem_step, 1)
            dve.wait_ge(dem_step, 6)
            nc.vector.transpose(dem[:, :, :].rearrange("p c b -> p (c b)"), dem_q[:, :]).then_inc(dem_step, 1)
            dve.wait_ge(dem_step, 7)
            scale_y(first, 0)
            sum_x1(dve, first, 0)
            turn_x(second, 0)
            for c in range(NC):
                if c + 1 < NC:
                    scale_y(first, c + 1)
                    sum_x1(dve, first, c + 1)
                x1_low(dve, first, c)
                if c + 1 < NQ:
                    turn_x(second, c + 1)
            scale_x(dve, second, 0)
            scale_x(dve, second, 1)
            for c in range(NC):
                xs_low(dve, second, c)
                if c + 2 < NC:
                    scale_x(dve, second, c + 2)
                turn_xwb(first, c)
            schedule(dve, window, first=0)
            turn_out((0, NB - 1), NQ - 1)

        @block.tensor
        def _(pe):
            def passes(ps, w_hi, w_lo, a_hi, a_lo, c, k):
                yield ps[:, :], w_lo[:, k, c], a_hi[:, k], k == 0, False
                yield ps[:, :], w_hi[:, k, c], a_lo[:, k], False, False
                yield ps[:, :], w_hi[:, k, c], a_hi[:, k], False, k == NC - 1

            def y_chunk(m, c):
                if y_bank(m, c) is y_ps[c % 2]:
                    wait(pe, yd_done, upto(NC, m, c - 1))
                for k in range(NC):
                    if c == 0:
                        pe.wait_ge(xs_lo_done, upto(NC, m, k + 1))
                        if is_block_0(m):
                            pe.wait_ge(w0_lo_done, k + 1)
                    for ps, w, a, first, last in passes(y_bank(m, c), w0_hi, w0_lo, xs_hi, xs_lo, c, k):
                        mm = nc.tensor.matmul(ps, w, a, start=first, stop=last)
                        if last:
                            mm.then_inc(y_done, 1)
                        yield

            def xw_chunks(m, parts):
                for c, k in parts:
                    if c == 0:
                        pe.wait_ge(x1_lo_done, upto(NC, m, k + 1))
                        if is_block_0(m):
                            pe.wait_ge(wx_lo_done, k + 1)
                    if k == 0:
                        wait(pe, xwb_done, upto(NC, m, c - 3))
                        if is_block_0(m) and c >= 2:
                            pe.wait_ge(yd_done, c + 1)
                    for ps, w, a, first, last in passes(xw_ps[c], wx_hi, wx_lo, x1_hi, x1_lo, c, k):
                        mm = nc.tensor.matmul(ps, w, a, start=first, stop=last)
                        if last:
                            mm.then_inc(xw_done, 1)
                        yield

            def chain(n, t):
                pe.wait_ge(h_turned, upto(STEPS, n, t + 1))
                if is_block_0(n) and t == 0:
                    pe.wait_ge(wh_in, NJ * DMA)
                for k in range(NC):
                    for j in range(NJ):
                        mm = nc.tensor.matmul(z[t % 2][G * j:G * j + G, 0:128], h_t[:, (t - 1) % STEPS, k],
                                              wh_sb[:, k, 128 * j:128 * j + 128], start=(k == 0), stop=(k == NC - 1))
                mm.then_inc(z_product, 1)

            XW_PARTS = [(0, 0), (0, 1), (1, 0), (1, 1), (0, 2), (1, 2), (0, 3), (1, 3)] + \
                       [(c, k) for c in (2, 3) for k in range(NC)]

            PER_STEP = 2 * 3 * NC * NC // STEPS
            WARM = 3

            def keep_warm(count):
                for _ in range(count):
                    nc.tensor.matmul(y_ps[0][:, :], w0_hi[:, 0, 0], xs_hi[:, 0], start=True, stop=True)

            def fill(n):
                ahead, next_ = blk(n, 2), blk(n, 1)
                if exists(next_):
                    for c in range(1, NC):
                        yield from y_chunk(next_, c)
                    yield from xw_chunks(next_, XW_PARTS)
                if exists(ahead):
                    yield from y_chunk(ahead, 0)

            def window(n):
                products = fill(n)
                for t in range(STEPS):
                    if exists(n):
                        chain(n, t)
                    filled = 0
                    while filled < PER_STEP and next(products, True) is None:
                        filled += 1
                    if filled < WARM and exists(n) and t < STEPS - 1:
                        keep_warm(WARM - filled)
                for _ in products:
                    pass

            pe.wait_ge(ys_done, 2)
            pe.wait_ge(w0_squared, NC)
            for k in range(NC):
                for j in range(NJ):
                    mm = nc.tensor.matmul(xw_ps[0][G * j:G * j + G, 0:128], ys2[:, k],
                                          w0_sq[:, k, 128 * j:128 * j + 128], start=(k == 0), stop=(k == NC - 1))
            mm.then_inc(dem_summed, 1)
            for _ in y_chunk((0, 0), 0):
                pass
            schedule(pe, window, first=-1)


_INS = ['x', 'cond_1024', 'L0_cond_weight', 'L1_cond_Wx', 'L1_cond_Wh', 'L1_cond_b']
_OUTS = [((32, 512, 512), 'float32')]


def kernel(**inputs):
    import numpy as _np
    import concourse.bacc as _bacc
    from concourse import mybir as _mybir
    from concourse.bass_utils import run_bass_kernel_spmd as _run

    nc = _bacc.Bacc("TRN2", target_bir_lowering=False, num_devices=1)
    arrays, args = {}, []
    for name in _INS:
        a = _np.ascontiguousarray(inputs[name])
        arrays[f"in_{name}_dram"] = a
        args.append(nc.dram_tensor(f"in_{name}_dram", a.shape, _mybir.dt.from_np(a.dtype), kind="ExternalInput").ap())
    for i, (shape, dtype) in enumerate(_OUTS):
        dt = _mybir.dt.from_np(_np.dtype(dtype))
        args.append(nc.dram_tensor(f"out_{i}_dram", shape, dt, kind="ExternalOutput").ap())
    build(nc, *args)
    r = _run(nc, [arrays], core_ids=[0])
    return r.results[0]["out_0_dram"]
```
